# Optimizing a Trainium2 kernel written in Bass

```python
import numpy as np
import jax
import jax.numpy as jnp

def _softmax(x, axis=-1):
    return jax.nn.softmax(x, axis=axis)

def _gelu(x):
    return jax.nn.gelu(x, approximate=True)

def _silu(x):
    return jax.nn.silu(x)

def _sigmoid(x):
    return jax.nn.sigmoid(x)

def _layernorm(x, axis=-1, eps=1e-05):
    m = jnp.mean(x, axis=axis, keepdims=True)
    v = jnp.var(x, axis=axis, keepdims=True)
    return (x - m) / jnp.sqrt(v + eps)

def _scatter_add(tgt, idx, src, axis=0):
    return tgt.at[idx].add(src)

def _segment_sum(src, seg, n):
    return jax.ops.segment_sum(src, seg, n)
kernel_name = 'mk_lm_tower_d1_tok_ids1024_r4_4436b9'

def setup_inputs(seed: int=0):
    np.random.seed(seed)
    _w = jnp.asarray

    def _rec_inputs():
        import jax
        import jax.numpy as jnp
        _rk = jax.random.key(seed)
        x = jax.random.randint(jax.random.fold_in(_rk, 1), (16, 512), 0, 12564, jnp.int32)
        return x
    x = _rec_inputs()

    def _L0_tok_setup():
        import jax, jax.numpy as jnp
        import numpy as np
        MAX_WORDS = 50257
        INPUT_SIZE = 256
        BATCH, SEQ = (8, 512)
        key = jax.random.key(seed)
        kx, kw, kb = jax.random.split(key, 3)
        x = jax.random.randint(kx, (BATCH, SEQ), 0, MAX_WORDS, dtype=jnp.int64 if jax.config.jax_enable_x64 else jnp.int32)
        W = jax.random.normal(kw, (INPUT_SIZE, MAX_WORDS), dtype=jnp.float32) * 0.02
        b = jax.random.normal(kb, (INPUT_SIZE,), dtype=jnp.float32) * 0.02
        return {'x': x, 'W': W, 'b': b}
    _L0_tok_all = _L0_tok_setup()
    _L0_tok_in = {k: v for k, v in _L0_tok_all.items() if k in ('W', 'b')}
    del _L0_tok_all

    def _L0_attn_setup():
        import jax, jax.numpy as jnp
        import numpy as np
        key = jax.random.key(seed)
        ks = jax.random.split(key, 8)
        B, L, DIM, INNER = (4, 1024, 256, 128)
        return {'x': jax.random.normal(ks[0], (B, L, DIM), dtype=jnp.float32), 'w_a': jax.random.normal(ks[1], (2 * INNER, DIM), dtype=jnp.float32) * DIM ** (-0.5), 'w_x': jax.random.normal(ks[2], (2 * INNER, DIM), dtype=jnp.float32) * DIM ** (-0.5), 'w_out': jax.random.normal(ks[3], (DIM, INNER), dtype=jnp.float32) * INNER ** (-0.5), 'mat_v_real': jax.random.normal(ks[4], (INNER, INNER), dtype=jnp.float32), 'mat_v_imag': jax.random.normal(ks[5], (INNER, INNER), dtype=jnp.float32), 'last_hidden_real': jax.random.normal(ks[6], (INNER,), dtype=jnp.float32), 'last_hidden_imag': jax.random.normal(ks[7], (INNER,), dtype=jnp.float32)}
    _L0_attn_all = _L0_attn_setup()
    _L0_attn_in = {k: v for k, v in _L0_attn_all.items() if k in ('w_a', 'w_x', 'w_out', 'mat_v_real', 'mat_v_imag', 'last_hidden_real', 'last_hidden_imag')}
    del _L0_attn_all

    def _L0_ffn_setup():
        import jax, jax.numpy as jnp
        import numpy as np
        ALPHA = 1.702
        LIMIT = 7.0
        EPS = 1e-05
        E = 16
        K = 4

        def _swiglu(h):
            x_glu = jnp.minimum(h[..., ::2], LIMIT)
            x_lin = jnp.clip(h[..., 1::2], LIMIT, LIMIT)
            return x_glu * jax.nn.sigmoid(ALPHA * x_glu) * (x_lin + 1.0)
        key = jax.random.key(seed)
        ks = jax.random.split(key, 7)
        B, T, H, I = (1, 512, 256, 256)
        x = jax.random.normal(ks[0], (B, T, H), jnp.float32)
        scale = jnp.ones((H,), jnp.float32)
        gate_w = jax.random.normal(ks[1], (E, H), jnp.float32) * 0.02
        gate_b = jnp.zeros((E,), jnp.float32)
        mlp1_w = jax.random.normal(ks[2], (E, 2 * I, H), jnp.float32) * 0.02
        mlp1_b = jax.random.normal(ks[3], (E, 2 * I), jnp.float32) * 0.02
        mlp2_w = jax.random.normal(ks[4], (E, H, I), jnp.float32) * 0.02
        mlp2_b = jax.random.normal(ks[5], (E, H), jnp.float32) * 0.02
        return dict(x=x, scale=scale, gate_w=gate_w, gate_b=gate_b, mlp1_w=mlp1_w, mlp1_b=mlp1_b, mlp2_w=mlp2_w, mlp2_b=mlp2_b)
    _L0_ffn_all = _L0_ffn_setup()
    _L0_ffn_in = {k: v for k, v in _L0_ffn_all.items() if k in ('scale', 'gate_w', 'gate_b', 'mlp1_w', 'mlp1_b', 'mlp2_w', 'mlp2_b')}
    del _L0_ffn_all
    return {'x': x, 'L0_tok_W': _L0_tok_in['W'], 'L0_tok_b': _L0_tok_in['b'], 'L0_attn_w_a': _L0_attn_in['w_a'], 'L0_attn_w_x': _L0_attn_in['w_x'], 'L0_attn_w_out': _L0_attn_in['w_out'], 'L0_attn_mat_v_real': _L0_attn_in['mat_v_real'], 'L0_attn_mat_v_imag': _L0_attn_in['mat_v_imag'], 'L0_attn_last_hidden_real': _L0_attn_in['last_hidden_real'], 'L0_attn_last_hidden_imag': _L0_attn_in['last_hidden_imag'], 'L0_ffn_scale': _L0_ffn_in['scale'], 'L0_ffn_gate_w': _L0_ffn_in['gate_w'], 'L0_ffn_gate_b': _L0_ffn_in['gate_b'], 'L0_ffn_mlp1_w': _L0_ffn_in['mlp1_w'], 'L0_ffn_mlp1_b': _L0_ffn_in['mlp1_b'], 'L0_ffn_mlp2_w': _L0_ffn_in['mlp2_w'], 'L0_ffn_mlp2_b': _L0_ffn_in['mlp2_b']}

def reference(x, L0_tok_W, L0_tok_b, L0_attn_w_a, L0_attn_w_x, L0_attn_w_out, L0_attn_mat_v_real, L0_attn_mat_v_imag, L0_attn_last_hidden_real, L0_attn_last_hidden_imag, L0_ffn_scale, L0_ffn_gate_w, L0_ffn_gate_b, L0_ffn_mlp1_w, L0_ffn_mlp1_b, L0_ffn_mlp2_w, L0_ffn_mlp2_b):
    import jax
    import jax.numpy as jnp

    def _L0_tok_ref(x, W, b):
        import jax, jax.numpy as jnp
        import numpy as np
        MAX_WORDS = 50257
        INPUT_SIZE = 256
        BATCH, SEQ = (8, 512)
        return jnp.take(W.T, x, axis=0) + b

    def _L0_attn_ref(x, w_a, w_x, w_out, mat_v_real, mat_v_imag, last_hidden_real, last_hidden_imag):
        import jax, jax.numpy as jnp
        import numpy as np
        b, l, dim = x.shape
        inner = mat_v_real.shape[0]
        V = jax.lax.complex(mat_v_real, mat_v_imag)
        Vinv = jnp.linalg.inv(V)
        h0 = jax.lax.complex(last_hidden_real, last_hidden_imag)
        xf = x.astype(jnp.float32)
        a2 = (xf @ w_a.T).reshape(b, l, inner, 2)
        a_mag2 = a2[..., 0] ** 2 + a2[..., 1] ** 2
        a = jax.lax.complex(a2[..., 0], a2[..., 1]) * (jax.lax.rsqrt(a_mag2) * jax.nn.sigmoid(jnp.log(a_mag2)))
        x2 = (xf @ w_x.T).reshape(b, l, inner, 2)
        x_mag2 = x2[..., 0] ** 2 + x2[..., 1] ** 2
        xc = jax.lax.complex(x2[..., 0], x2[..., 1]) * (jax.lax.rsqrt(x_mag2) * x_mag2)
        x_roll = jnp.concatenate([jnp.broadcast_to(h0, (b, 1, inner)), xc[:, :-1]], axis=1)
        u = jnp.einsum('mn,bln->blm', Vinv, x_roll)

        def combine(c1, c2):
            a1, b1 = c1
            a2_, b2 = c2
            return (a2_ * a1, a2_ * b1 + b2)
        _, s = jax.lax.associative_scan(combine, (a, a * u), axis=1)
        h = jnp.einsum('mn,bln->blm', V, s) + xc
        return (h.real @ w_out.T).astype(x.dtype)

    def _L0_ffn_ref(x, scale, gate_w, gate_b, mlp1_w, mlp1_b, mlp2_w, mlp2_b):
        import jax, jax.numpy as jnp
        import numpy as np
        ALPHA = 1.702
        LIMIT = 7.0
        EPS = 1e-05
        E = 16
        K = 4

        def _swiglu(h):
            x_glu = jnp.minimum(h[..., ::2], LIMIT)
            x_lin = jnp.clip(h[..., 1::2], LIMIT, LIMIT)
            return x_glu * jax.nn.sigmoid(ALPHA * x_glu) * (x_lin + 1.0)
        t = x * jax.lax.rsqrt(jnp.mean(x * x, axis=-1, keepdims=True) + EPS) * scale
        g = jnp.einsum('bth,eh->bte', t, gate_w) + gate_b
        vals, idx = jax.lax.top_k(g, K)
        w = jax.nn.softmax(vals, axis=-1)
        route = jnp.sum(jax.nn.one_hot(idx, E, dtype=t.dtype) * w[..., None], axis=-2)
        route_e = jnp.moveaxis(route, -1, 0)

        def step(acc, p):
            w1, b1, w2, b2, r = p
            h = jnp.einsum('bth,ih->bti', t, w1) + b1
            s = _swiglu(h)
            y = jnp.einsum('bti,hi->bth', s, w2) + b2
            return (acc + r[..., None] * y, None)
        acc, _ = jax.lax.scan(step, jnp.zeros_like(x), (mlp1_w, mlp1_b, mlp2_w, mlp2_b, route_e))
        return x + acc
    h = _L0_tok_ref(x, L0_tok_W, L0_tok_b)
    h = h + _L0_attn_ref(_layernorm(h, axis=-1), L0_attn_w_a, L0_attn_w_x, L0_attn_w_out, L0_attn_mat_v_real, L0_attn_mat_v_imag, L0_attn_last_hidden_real, L0_attn_last_hidden_imag)
    h = h + _L0_ffn_ref(_layernorm(h, axis=-1), L0_ffn_scale, L0_ffn_gate_w, L0_ffn_gate_b, L0_ffn_mlp1_w, L0_ffn_mlp1_b, L0_ffn_mlp2_w, L0_ffn_mlp2_b)
    return h

_drawn_inputs = setup_inputs


def setup_inputs(seed=0):
    import zlib

    import numpy as np

    out = dict(_drawn_inputs(seed))
    spreads = {'L0_ffn_scale': (1.0, 0.6), 'L0_ffn_gate_b': (0.0, 0.8)}
    factors = {'L0_attn_last_hidden_real': 32.338,
     'L0_attn_last_hidden_imag': 40.813,
     'L0_ffn_gate_w': 8.0,
     'L0_ffn_mlp1_w': 8.0,
     'L0_ffn_mlp1_b': 52.504,
     'L0_ffn_mlp2_w': 8.0,
     'L0_ffn_mlp2_b': 64.0}
    for name, (base, spread) in spreads.items():
        noise = np.random.default_rng([zlib.crc32(name.encode()), seed]).standard_normal(out[name].shape)
        drawn = base * np.exp(spread * noise) if base else spread * noise
        out[name] = jnp.asarray(drawn.astype(out[name].dtype))
    for name, factor in factors.items():
        out[name] = (out[name] * factor).astype(out[name].dtype)
    return out
```

```python
from contextlib import ExitStack

import concourse.bass as bass
from concourse import mybir

F32 = mybir.dt.float32
BF16 = mybir.dt.bfloat16
F16 = mybir.dt.float16
I32 = mybir.dt.int32
U32 = mybir.dt.uint32
ALU = mybir.AluOpType
ACT = mybir.ActivationFunctionType
AXX = mybir.AxisListType.X

P = 128
PI = 3.14159265358979
MAGIC = 12582912.0
EPS = 1e-5
LIMIT = 7.0
BIG = 3.0e38


def newton_scales(lowest=1e-14, largest=1.98):
    low, scales = lowest, []
    while 1 - low > 1e-7:
        c = min(2 / (1 + low), largest)
        low = min(c * low * (2 - c * low), c * (2 - c))
        scales.append(c)
    return scales + [1.0, 1.0]


def need(eng, sem, value):
    if not isinstance(value, int) or value > 0:
        eng.wait_ge(sem, value)


def layer_kernel(nc, x, tok_W, tok_b, w_a, w_x, w_out, v_re, v_im, h0_re, h0_im,
                 scale, gate_w, gate_b, mlp1_w, mlp1_b, mlp2_w, mlp2_b, out):
    D = tok_W.shape[1]
    NT = x.shape[1]
    NI = v_re.shape[0]
    E = gate_b.shape[0]
    L = 512
    TPC = L // P
    C = NT // TPC
    KT = D // P

    I = mlp2_w.shape[1]
    K = 4
    TILES = NT * K + E
    QUARTERS = 4
    assert I == D and NT // QUARTERS * P <= 2048 and TILES % 4 == 0

    scales = newton_scales()
    first = scales[0]
    same = sum(1 for c in scales if c == first)
    assert all(c == first for c in scales[:same]) and same > C

    with ExitStack() as ctx:
        def sb(name, shape, dt=F32):
            return ctx.enter_context(nc.sbuf_tensor(name, shape, dt))

        def sem(name):
            return ctx.enter_context(nc.semaphore(name))

        H = sb("H", [P, NT, D])
        ids = sb("ids", [P, NT], I32)
        stats = sb("stats", [P, NT, 2])
        rstd = sb("rstd", [P, NT])
        std = sb("std", [P, NT])
        ident = sb("ident", [P, P])
        ones = sb("ones", [P, P])
        eps = sb("eps", [P, 1])
        half_pi = sb("half_pi", [P, 1])
        tiny = sb("tiny", [P, 1])

        arena = sb("arena", [P, 31400])
        used = [0]

        def take(*shape):
            size = 1
            for s in shape:
                size *= s
            a = used[0]
            used[0] += size
            assert used[0] <= 31400
            ap = arena[:, a:a + size]
            if len(shape) == 2:
                ap = ap.rearrange("p (a b) -> p a b", a=shape[0])
            elif len(shape) == 3:
                ap = ap.rearrange("p (a b c) -> p a b c", a=shape[0], b=shape[1])
            return ap

        W_ax = take(KT, 4, NI)
        W_o = take(D)
        VT = take(3, NI)
        Y = take(3, NI)
        rows = [take(TPC, D) for _ in range(2)]
        rowsT = [take(KT, L) for _ in range(2)]
        zeros = take(L)
        at = used[0]
        bias_rows = take(TPC, D)
        v_nat = take(2, NI)
        X = take(2, NI)
        Z = take(3, NI)
        two_i = take(2, NI)
        sq_junk = take(NI)
        frob = take(4)
        used[0] = at
        sq_ar, sq_ai, sq_xr, sq_xi = (take(L) for _ in range(4))
        m_a, m_x, rho, g_x = (take(L) for _ in range(4))
        m1, srho, den, aim, prod, rec, tan_h = (take(L) for _ in range(7))
        half = take(L)
        r1, r2 = take(L), take(L)
        decay = [take(L) for _ in range(2)]
        phi, turns, angle, mag = take(L + 1), take(L), take(L + 1), take(L + 1)
        cosE = [take(L + 1) for _ in range(2)]
        sinE = [take(L + 1) for _ in range(2)]
        xc_re = [take(L + 1) for _ in range(2)]
        xc_im = [take(L + 1) for _ in range(2)]
        c_ur, s_ui, c_ui, s_ur = (take(L) for _ in range(4))
        w_re, w_im, z_re, z_im = (take(L) for _ in range(4))
        c_zr, s_zi, s_zr, c_zi = c_ur, s_ui, c_ui, s_ur
        s_re, s_im, h_re = (take(L) for _ in range(3))
        idx = [sb(f"idx{i}", [P, TPC], I32) for i in range(2)]
        st6 = sb("st6", [P, TPC, 6])
        mv = sb("mv", [P, TPC, 2])

        used[0] = 0
        W_up = take(E, KT, I)
        W_dn = take(E, KT, D)
        b_up = take(E, I)
        at = used[0]
        entry = [take(TPC, D + E) for _ in range(2)]
        tT = [take(KT, L) for _ in range(2)]
        acc_row = [take(TPC, D) for _ in range(2)]
        routeT = take(TPC * P)[0:E, :]
        found = take(3, TILES)
        expert_f = take(3, TILES)
        HOTS = 4
        hot_lo = [take(P // 2).bitcast(F16) for i in range(HOTS)]
        hot_hi = [take(TILES // 2).bitcast(F16) for i in range(HOTS)]
        slots_i = take(3, NT * K).bitcast(I32)
        slots, slot_lo, slot_hi = (take(NT * K) for _ in range(3))
        used[0] = at
        total, upto, slot, order, picked = (take(NT * E) for _ in range(5))
        used[0] = at
        RING = 4
        AHEAD = 5
        XRING = 8
        x_in = [take(D + E) for _ in range(XRING)]
        y_out = [take(D) for _ in range(RING)]
        xT = [take(KT, P) for _ in range(2)]
        hid = [take(I) for _ in range(2)]
        act_h = [take(I) for _ in range(2)]
        actT = [take(KT, P) for _ in range(2)]

        stats2 = sb("stats2", [P, NT, 2])
        std2 = sb("std2", [P, 2, NT])
        rstd2 = sb("rstd2", [P, 4, NT])
        mask = sb("mask", [P, NT * E], BF16)
        logit = sb("logit", [P, TPC, E + 4])
        left = sb("left", [P, TPC, E + 4])
        top8 = sb("top8", [P, TPC, 8])
        top4 = sb("top4", [P, TPC, 8])
        expd = sb("expd", [P, TPC, E])
        expm = sb("expm", [P, TPC, E])
        sums = sb("sums", [P, 2, TPC])
        gate = sb("gate", [P, KT, E])
        gate_bias = sb("gate_bias", [P, E])
        b_dn = sb("b_dn", [E, D])
        scale_col = sb("scale_col", [P, KT])
        lower = sb("lower", [P, P], BF16)
        ones16 = sb("ones16", [P, P], BF16)
        iota_t = sb("iota_t", [P, TILES], I32)
        iota_tf = sb("iota_tf", [P, TILES])
        iota_hi = sb("iota_hi", [P, TILES], F16)
        iota_lo = sb("iota_lo", [P, P], F16)
        value = sb("value", [P, NT // QUARTERS])
        keep = sb("keep", [P, 2, NT * E], BF16)
        tiles_e = sb("tiles_e", [P, 4, E])
        slot_token = sb("slot_token", [P, TILES], I32)
        tile_expert = sb("tile_expert", [P, TILES], I32)
        tile_starts = sb("tile_starts", [P, TILES], I32)
        tok = [sb(f"tok{i}", [P, 1], I32) for i in range(XRING)]

        A = ctx.enter_context(nc.psum_tensor("A", [P, 2 * L], F32))
        B = ctx.enter_context(nc.psum_tensor("B", [P, 4 * L], F32))
        Cb = ctx.enter_context(nc.psum_tensor("Cb", [P, 2 * L], F32))
        a_re, a_im, x_re, x_im = (B[:, g * L:(g + 1) * L] for g in range(4))
        u_re, u_im = Cb[:, 0:L], Cb[:, L:2 * L]
        T_ps, X_ps, Y_ps, N_ps = (B[:, g * L:g * L + 2 * NI] for g in range(4))
        VT_ps = A[:, 0:2 * NI]
        logit_ps, rT_ps = B[:, 0:TPC * E], B[0:E, L:2 * L]
        xT_ps = [A[:, i * L:i * L + D] for i in range(2)]
        up_ps = [Cb[:, i * L:i * L + I] for i in range(2)]
        aT_ps = [B[:, i * L:i * L + I] for i in range(2)]
        dn_ps = [B[:, (2 + i) * L:(2 + i) * L + D] for i in range(2)]

        S = {k: sem(k) for k in (
            "ids_in v_in w_in h0_in bias_in const_set frob_sum frob_ps vt_ps vt_ready x0_ready "
            "y0_ready t_ps z_ready zn_ready x_ps y_ps x_ready y_ready idx_ready h_ready st_ready mv_ready std_ready "
            "rstd_ready xn_ready xt_ps xt_ready proj sqa_ready sqx_ready ma_ready mx_ready rho_ready gx_ready "
            "m1_ready srho_ready den_ready aim_ready prod_ready rec_ready tan_ready atan_ready phi_ready turns_ready "
            "npi_ready sum_ready angle_ready mag_ready sin_ready cos_ready xc_ready r1_ready r2_ready decay_ready "
            "dve_step apart ag_ready ag2_ready consts2 stat2_ready mv2_ready r_std r_c r_d gate_in weights_in "
            "entry_ready tT_ps tT_ready gate_ps logit_ready top8_ready top4_ready left_ready mask_ready diff_ready "
            "exp_ready expm_ready esum_ready erec_ready route_ready rT_ps rT_ready bd_ps acc_ready "
            "zero_rows part_ready iota_ready lowps totps "
            "slot_c slot_ready hotlo_ready hothi_ready hot_used "
            "tok_ready e_d expert_ready up_scaled tokc_ready "
            "xT_ps xT_ready up_ps hid_a hid_ready act_ready aT_ps aT_ready dn_ps y_ready2 "
            "u_ps rot_ready w_ready z_ready2 back_ready s_ready hr_ps h_re_ready o_ps h2_ready").split()}
        gathered = [sem(f"gathered{i}") for i in range(2)]
        table_in = [sem(f"table_in{i}") for i in range(2)]
        acc_in = [sem(f"acc_in{i}") for i in range(2)]
        fetched = [sem(f"fetched{i}") for i in range(XRING)]
        scattered = [sem(f"scattered{i}") for i in range(RING)]
        table = nc.dram_tensor("table", (NT * P + P, D + E), F32, kind="Internal").ap()
        table_v = table.rearrange("(j p) d -> p j d", p=P)
        out_v = out.rearrange("(j p) d -> p j d", p=P)
        block = ctx.enter_context(nc.Block())

        def sweep(eng, body, steps, head, tail, w=2):
            for n in range(head):
                body(n, n % w)
            with eng.Fori(head // w, (steps - tail) // w) as i:
                for u in range(w):
                    body(w * i + u, u)
            for n in range(steps - tail, steps):
                body(n, n % w)

        def apart(eng):
            eng.sem_inc(S["apart"], 1)

        def bound(t, u):
            return (t - u) * 4

        def live(n):
            return not isinstance(n, int) or 0 <= n < C

        @block.sync
        def _(sp):
            sp.dma_start(v_nat[:, 0, :], v_re).then_inc(S["v_in"], 16)
            sp.dma_start(v_nat[:, 1, :], v_im).then_inc(S["v_in"], 16)
            sp.dma_start(ids[:, :], x).then_inc(S["ids_in"], 16)
            for i in range(TPC):
                sp.dma_start(bias_rows[:, i, :], tok_b.partition_broadcast(P)).then_inc(S["bias_in"], 16)
            sp.dma_start(W_ax[:, :, 0:2, :].rearrange("p t c n -> p t (c n)"),
                         w_a.rearrange("(t k) c n -> k t (c n)", k=P)).then_inc(S["w_in"], 16)
            sp.dma_start(W_ax[:, :, 2:4, :].rearrange("p t c n -> p t (c n)"),
                         w_x.rearrange("(t k) c n -> k t (c n)", k=P)).then_inc(S["w_in"], 16)
            sp.dma_start(W_o, w_out).then_inc(S["w_in"], 16)
            sp.wait_ge(S["y_ready"], 2 * len(scales))
            sp.wait_ge(S["h_ready"], C)
            for i in range(2):
                sp.dma_start(xc_re[i][:, 0:1], h0_re).then_inc(S["h0_in"], 16)
                sp.dma_start(xc_im[i][:, 0:1], h0_im).then_inc(S["h0_in"], 16)
            sp.dma_start(gate[:, :, :], gate_w.rearrange("(t k) e -> k t e", k=P)).then_inc(S["gate_in"], 16)
            sp.dma_start(gate_bias[:, :], gate_b.partition_broadcast(P)).then_inc(S["gate_in"], 16)
            sp.dma_start(scale_col[:, :], scale).then_inc(S["gate_in"], 16)
            sp.dma_start(b_dn[:, :], mlp2_b).then_inc(S["gate_in"], 16)
            sp.wait_ge(S["h2_ready"], C)
            for t in range(KT):
                sp.dma_start(W_up[:, :, t, :], mlp1_w[:, t * P:(t + 1) * P, 0, :].rearrange("e k i -> k e i"))\
                    .then_inc(S["weights_in"], 16)
                sp.dma_start(W_dn[:, :, t, :], mlp2_w[:, t * P:(t + 1) * P, :].rearrange("e k i -> k e i"))\
                    .then_inc(S["weights_in"], 16)
            sp.dma_start(b_up, mlp1_b[:, 0, :].partition_broadcast(P)).then_inc(S["weights_in"], 16)
            sp.wait_ge(S["consts2"], 1)
            sp.dma_start(table_v[:, NT, :], found[:, 0, :]).then_inc(S["zero_rows"], 16)
            sp.dma_start(out_v[:, NT, :], found[:, 0, 0:D]).then_inc(S["zero_rows"], 16)

            def store(c, par):
                sp.wait_ge(S["route_ready"], c + 1)
                sp.dma_start(table_v[:, bass.ds(c * TPC, TPC), :], entry[par]).then_inc(table_in[par], 16)
                sp.wait_ge(S["acc_ready"], c + 1)
                sp.dma_start(out_v[:, bass.ds(c * TPC, TPC), :], acc_row[par]).then_inc(acc_in[par], 16)

            sweep(sp, store, C, 2, 0)

        @block.gpsimd
        def _(pool):
            pool.memset(ident[:, :], 0.0).then_inc(S["const_set"], 1)
            pool.memset(ones[:, :], 1.0).then_inc(S["const_set"], 1)
            pool.memset(two_i, 0.0).then_inc(S["const_set"], 1)
            pool.memset(eps[:, :], EPS).then_inc(S["const_set"], 1)
            pool.memset(half_pi[:, :], PI / 2).then_inc(S["const_set"], 1)
            pool.memset(tiny[:, :], 1e-37).then_inc(S["const_set"], 1)
            pool.memset(zeros, 0.0).then_inc(S["const_set"], 1)
            pool.wait_ge(S["const_set"], 7)
            pool.affine_select(out=ident[:, :], in_=ident[:, :], compare_op=ALU.not_equal, fill=1.0,
                               base=0, pattern=[[-1, P]], channel_multiplier=1).then_inc(S["const_set"], 1)
            pool.affine_select(out=two_i[:, 0, :], in_=two_i[:, 0, :], compare_op=ALU.not_equal, fill=2.0,
                               base=0, pattern=[[-1, P]], channel_multiplier=1).then_inc(S["const_set"], 1)

            pool.wait_ge(S["ids_in"], 16)

            def gather(c, par):
                if not isinstance(c, int):
                    pool.wait_ge(gathered[par], (c - par) * 8 * TPC)
                    pool.wait_ge(S["h_ready"], c - 1)
                pool.tensor_copy(idx[par][:, :], ids[:, bass.ds(c * TPC, TPC)]).then_inc(S["idx_ready"], 1)
                pool.wait_ge(S["idx_ready"], c + 1)
                apart(pool)
                for i in range(TPC):
                    pool.indirect_dma_start(
                        rows[par][:, i, :], None, tok_W,
                        bass.IndirectOffsetOnAxis(ap=idx[par][:, i:i + 1], axis=0)).then_inc(gathered[par], 16)

            sweep(pool, gather, C, 2, 0)

            pool.wait_ge(S["y_ready"], 2 * len(scales))
            pool.memset(phi[:, 0:1], 0.0).then_inc(S["const_set"], 1)

            def add(out_, a, b, done):
                pool.tensor_tensor(out_, a, b, ALU.add).then_inc(S[done], 1)

            def step(n, par):
                if live(n):
                    pool.wait_ge(S["sqa_ready"], 2 * n + 2)
                    need(pool, S["rho_ready"], n)
                    need(pool, S["m1_ready"], n)
                    add(m_a, sq_ar, sq_ai, "ma_ready")
                    pool.wait_ge(S["sqx_ready"], 2 * n + 2)
                    need(pool, S["gx_ready"], n)
                    add(m_x, sq_xr, sq_xi, "mx_ready")
                if live(n - 2):
                    pool.wait_ge(S["back_ready"], 4 * (n - 2) + 4)
                    need(pool, S["hr_ps"], n - 2)
                    pool.tensor_tensor(s_re, c_zr, s_zi, ALU.subtract).then_inc(S["s_ready"], 1)
                    add(s_im, s_zr, c_zi, "s_ready")
                if live(n):
                    pool.wait_ge(S["srho_ready"], n + 1)
                    pool.wait_ge(S["rho_ready"], n + 1)
                    pool.tensor_tensor(r1, srho, rho, ALU.mult).then_inc(S["r1_ready"], 1)
                    pool.wait_ge(S["r1_ready"], n + 1)
                    pool.wait_ge(S["den_ready"], n + 1)
                    pool.tensor_tensor(r2, r1, den, ALU.mult).then_inc(S["r2_ready"], 1)
                    pool.wait_ge(S["r2_ready"], n + 1)
                    pool.wait_ge(S["rec_ready"], n + 1)
                    need(pool, S["z_ready2"], 2 * (n - 1))
                    pool.tensor_tensor(decay[par], r2, rec, ALU.mult).then_inc(S["decay_ready"], 1)
                if live(n - 1):
                    pool.wait_ge(S["rot_ready"], 4 * (n - 1) + 4)
                    need(pool, S["z_ready2"], 2 * (n - 1))
                    add(w_re, c_ur, s_ui, "w_ready")
                    pool.tensor_tensor(w_im, c_ui, s_ur, ALU.subtract).then_inc(S["w_ready"], 1)

            sweep(pool, step, C + 2, 4, 2)

            pool.wait_ge(S["h2_ready"], C)
            pool.memset(found[:, 0, :], 0.0).then_inc(S["consts2"], 1)
            pool.memset(lower[:, :], 1.0).then_inc(S["iota_ready"], 1)
            pool.memset(ones16[:, :], 1.0).then_inc(S["iota_ready"], 1)
            pool.memset(logit[:, :, :], BIG).then_inc(S["iota_ready"], 1)
            pool.memset(top4[:, :, :], BIG).then_inc(S["iota_ready"], 1)
            pool.memset(keep[:, :, :], 1.0).then_inc(S["iota_ready"], 1)
            pool.iota(iota_t[:, :], [[1, TILES]], base=0, channel_multiplier=0).then_inc(S["iota_ready"], 1)
            pool.iota(slots_i[:, 0, 0:NT // QUARTERS], [[P, NT // QUARTERS]], base=1, channel_multiplier=1)\
                .then_inc(S["iota_ready"], 1)
            pool.wait_ge(S["iota_ready"], 7)
            pool.affine_select(out=lower[:, :], in_=lower[:, :], compare_op=ALU.is_gt, fill=0.0, base=0,
                               pattern=[[1, P]], channel_multiplier=-1).then_inc(S["iota_ready"], 1)
            pool.memset(keep[:, 0, :].rearrange("p (e j) -> p e j", e=E)[:, :, 0:1], 0.0)\
                .then_inc(S["iota_ready"], 1)
            pool.memset(keep[:, 1, :].rearrange("p (j e) -> p j e", e=E)[:, :, 0:1], 0.0)\
                .then_inc(S["iota_ready"], 1)
            pool.tensor_copy(iota_hi[:, :], iota_t[:, :]).then_inc(S["iota_ready"], 1)
            pool.tensor_copy(iota_tf[:, :], iota_t[:, :]).then_inc(S["iota_ready"], 1)
            pool.tensor_copy(iota_lo[:, :], iota_t[:, 0:P]).then_inc(S["iota_ready"], 1)
            pool.tensor_copy(value[:, :], slots_i[:, 0, 0:NT // QUARTERS]).then_inc(S["iota_ready"], 1)

            pool.wait_ge(S["weights_in"], 16 * (2 * KT + 1))
            pool.wait_ge(S["gate_in"], 64)
            for t in range(KT):
                w = W_up[:, :, t, :]
                pool.tensor_scalar(w, w, scale_col[:, t:t + 1], None, ALU.mult).then_inc(S["up_scaled"], 1)

            def add_residual(c, par):
                pool.wait_ge(S["part_ready"], TPC * (c + 1))
                pool.tensor_tensor(acc_row[par], acc_row[par], H[:, bass.ds(c * TPC, TPC), :], ALU.add)\
                    .then_inc(S["acc_ready"], 1)

            sweep(pool, add_residual, C, 2, 0)

            def fetch(t, u):
                need(pool, scattered[u % RING], bound(t, u % RING) - 16)
                pool.tensor_copy(tok[u][:, :], slot_token[:, bass.ds(t, 1)]).then_inc(S["tokc_ready"], 1)
                pool.wait_ge(S["tokc_ready"], t + 1)
                apart(pool)
                pool.indirect_dma_start(x_in[u], None, table, bass.IndirectOffsetOnAxis(ap=tok[u][:, 0:1], axis=0))\
                    .then_inc(fetched[u], 16)

            def scatter(t, u):
                if not isinstance(t, int) or t > 0:
                    starts = pool.value_load(tile_starts[0:1, bass.ds(t, 1)], min_val=0, max_val=1)
                    for back in range(1, RING):
                        if isinstance(t, int) and t - back < 0:
                            continue
                        v = (u - back) % RING
                        count = (t - back - v) * 4 + 16
                        pool.wait_ge(scattered[v], starts * (count - 16) + 16)
                pool.wait_ge(S["y_ready2"], t + 1)
                apart(pool)
                pool.indirect_dma_start(out, bass.IndirectOffsetOnAxis(ap=tok[u][:, 0:1], axis=0),
                                        y_out[u % RING], None, compute_op=ALU.add).then_inc(scattered[u % RING], 16)

            def expert(t, u):
                if not isinstance(t, int) or t + AHEAD < TILES:
                    fetch(t + AHEAD, (u + AHEAD) % XRING)
                scatter(t, u)

            pool.wait_ge(S["tok_ready"], 1)
            pool.wait_ge(S["expert_ready"], 2)
            pool.wait_ge(S["zero_rows"], 32)
            for i in range(2):
                pool.wait_ge(table_in[i], 8 * C)
                pool.wait_ge(acc_in[i], 8 * C)
            for t in range(AHEAD):
                fetch(t, t)
            sweep(pool, expert, TILES, XRING, XRING, XRING)
            for u in range(RING):
                pool.wait_ge(scattered[u], 16 * (TILES // RING))

        @block.tensor
        def _(pe):
            def cmul(out_, lhs, rhs, done):
                pe.matmul(out_, lhs[:, 0, :], rhs[:, 0:2, :].rearrange("p a b -> p (a b)"),
                          start=True, stop=False, skip_group_check=True)
                pe.matmul(out_[:, 0:NI], lhs[:, 2, :], rhs[:, 1, :], start=False, stop=False,
                          skip_group_check=True)
                pe.matmul(out_[:, NI:2 * NI], lhs[:, 1, :], rhs[:, 0, :], start=False, stop=True,
                          skip_group_check=True).then_inc(S[done], 1)

            pe.wait_ge(S["v_in"], 32)
            pe.wait_ge(S["const_set"], 9)
            for i in range(2):
                pe.transpose(VT_ps[:, i * NI:(i + 1) * NI], v_nat[:, i, :], ident[:, :]).then_inc(S["vt_ps"], 1)
            pe.wait_ge(S["frob_sum"], 1)
            pe.matmul(N_ps[:, 0:1], ones[:, :], frob[:, 2:3], start=True, stop=True).then_inc(S["frob_ps"], 1)
            pe.wait_ge(S["vt_ready"], 3)
            pe.wait_ge(S["x0_ready"], 2)
            pe.wait_ge(S["y0_ready"], 3)

            def newton(k):
                if not isinstance(k, int) or k > 0:
                    pe.wait_ge(S["x_ready"], k)
                cmul(T_ps, VT, X, "t_ps")
                pe.wait_ge(S["z_ready"], k + 1)
                pe.wait_ge(S["zn_ready"], k + 1)
                if not isinstance(k, int) or k > 0:
                    pe.wait_ge(S["y_ready"], 2 * k)
                cmul(X_ps, Y, Z, "x_ps")
                cmul(Y_ps, Z, Y, "y_ps")

            newton(0)
            with pe.Fori(1, same) as k:
                newton(k)
            for k in range(same, len(scales)):
                newton(k)

            def transposes(n, par):
                pe.wait_ge(S["xn_ready"], TPC * (n + 1))
                need(pe, S["h2_ready"], n - 3)
                for i in range(TPC):
                    for t in range(KT):
                        mm = pe.transpose(A[:, t * L + i * P:t * L + (i + 1) * P],
                                          rows[par][:, i, t * P:(t + 1) * P], ident[:, :])
                mm.then_inc(S["xt_ps"], 1)

            def project(n, par):
                pe.wait_ge(S["xt_ready"], KT * (n + 1))
                need(pe, S["aim_ready"], n)
                need(pe, S["sqa_ready"], 2 * n)
                need(pe, S["srho_ready"], n)
                need(pe, S["den_ready"], n)
                for g in range(4):
                    if g == 2:
                        need(pe, S["xc_ready"], 2 * n)
                        need(pe, S["sqx_ready"], 2 * n)
                    for t in range(KT):
                        mm = pe.matmul(B[:, g * L:(g + 1) * L], W_ax[:, t, g, :], rowsT[par][:, t, :],
                                       start=(t == 0), stop=(t == KT - 1))
                    mm.then_inc(S["proj"], 1)

            def inputs(n, par):
                pe.wait_ge(S["xc_ready"], 2 * n + 2)
                need(pe, S["rot_ready"], 4 * n)
                xr, xi = xc_re[par][:, 0:L], xc_im[par][:, 0:L]
                pe.matmul(u_re, Y[:, 0, :], xr, start=True, stop=False)
                pe.matmul(u_re, Y[:, 2, :], xi, start=False, stop=True)
                pe.matmul(u_im, Y[:, 0, :], xi, start=True, stop=False)
                pe.matmul(u_im, Y[:, 1, :], xr, start=False, stop=True).then_inc(S["u_ps"], 1)

            def real_part(n):
                pe.wait_ge(S["s_ready"], 2 * n + 2)
                pe.matmul(A[:, 0:L], VT[:, 0, :], s_re, start=True, stop=False)
                pe.matmul(A[:, 0:L], VT[:, 2, :], s_im, start=False, stop=True).then_inc(S["hr_ps"], 1)

            def project_out(n):
                pe.wait_ge(S["h_re_ready"], n + 1)
                for i in range(TPC):
                    mm = pe.matmul(A[:, i * D:(i + 1) * D], h_re[:, i * P:(i + 1) * P], W_o,
                                   start=True, stop=True)
                mm.then_inc(S["o_ps"], 1)

            pe.wait_ge(S["w_in"], 48)
            pe.wait_ge(S["h0_in"], 64)
            pe.wait_ge(S["y_ready"], 2 * len(scales))
            transposes(0, 0)
            project(0, 0)

            def step(n, par):
                if live(n - 1):
                    inputs(n - 1, 1 - par)
                if live(n + 1) and not (isinstance(n, int) and n + 1 >= C):
                    transposes(n + 1, 1 - par)
                if live(n - 2):
                    if not isinstance(n, int) or n + 1 < C:
                        pe.wait_ge(S["xt_ready"], KT * (n + 2))
                    need(pe, S["h2_ready"], n - 2)
                    real_part(n - 2)
                    project_out(n - 2)
                if live(n + 1) and not (isinstance(n, int) and n + 1 >= C):
                    project(n + 1, 1 - par)

            sweep(pe, step, C + 2, 4, 4)

            def gate_rows(c, par):
                pe.wait_ge(S["entry_ready"], TPC * (c + 1))
                need(pe, S["tT_ready"], KT * c)
                if isinstance(c, int) and c == 0:
                    pe.wait_ge(S["h2_ready"], C)
                for i in range(TPC):
                    for t in range(KT):
                        mm = pe.transpose(A[:, t * L + i * P:t * L + (i + 1) * P],
                                          entry[par][:, i, t * P:(t + 1) * P], ident[:, :])
                mm.then_inc(S["tT_ps"], 1)
                pe.wait_ge(S["tT_ready"], KT * (c + 1))
                need(pe, S["logit_ready"], c)
                for i in range(TPC):
                    for t in range(KT):
                        mm = pe.matmul(logit_ps[:, i * E:(i + 1) * E], tT[par][:, t, i * P:(i + 1) * P],
                                       gate[:, t, :], start=(t == 0), stop=(t == KT - 1))
                mm.then_inc(S["gate_ps"], 1)

            def biases(c, par):
                pe.wait_ge(S["route_ready"], c + 1)
                need(pe, S["rT_ready"], c)
                for i in range(TPC):
                    mm = pe.transpose(rT_ps[:, i * P:(i + 1) * P], entry[par][:, i, D:D + E], ident[:, :])
                mm.then_inc(S["rT_ps"], 1)
                pe.wait_ge(S["rT_ready"], c + 1)
                need(pe, S["part_ready"], TPC * c)
                for i in range(TPC):
                    mm = pe.matmul(Cb[:, i * D:(i + 1) * D], routeT[:, i * P:(i + 1) * P], b_dn[:, :],
                                   start=True, stop=True)
                mm.then_inc(S["bd_ps"], 1)

            def routing(c, par):
                if not isinstance(c, int) or c > 0:
                    biases(c - 1, 1 - par)
                if not isinstance(c, int) or c < C:
                    gate_rows(c, par)

            pe.wait_ge(S["gate_in"], 64)
            sweep(pe, routing, C + 1, 2, 1)

            pe.wait_ge(S["mask_ready"], C)
            pe.wait_ge(S["iota_ready"], 14)
            pe.wait_ge(S["tT_ready"], KT * C)
            pe.wait_ge(S["logit_ready"], C)
            pe.wait_ge(S["rT_ready"], C)
            pe.wait_ge(S["part_ready"], TPC * C)
            for i in range(2):
                pe.matmul(A[:, i * L:(i + 1) * L], lower[:, :], mask[:, i * L:(i + 1) * L], start=True, stop=True)\
                    .then_inc(S["lowps"], 1)
                pe.matmul(Cb[:, i * L:(i + 1) * L], ones16[:, :], mask[:, i * L:(i + 1) * L], start=True, stop=True)\
                    .then_inc(S["totps"], 1)

            def put(q, par, bank, start=False, stop=False):
                pe.wait_ge(S["hotlo_ready"], q + 1)
                pe.wait_ge(S["hothi_ready"], q + 1)
                pe.matmul(bank, hot_lo[par][:, :], hot_hi[par][:, :], start=start, stop=stop,
                          skip_group_check=True).then_inc(S["hot_used"], 1)

            per = NT * K // QUARTERS
            for f in range(QUARTERS):
                bank = B[:, f * L:f * L + TILES]
                for u in range(HOTS):
                    put(f * per + u, u, bank, start=(u == 0))
                with pe.Fori(1, per // HOTS - 1) as i:
                    for u in range(HOTS):
                        put(f * per + HOTS * i + u, u, bank)
                for u in range(HOTS):
                    put((f + 1) * per - HOTS + u, u, bank, stop=(u == HOTS - 1))

            def turn_rows(t, par, u):
                pe.wait_ge(fetched[u], (t - u) * (16 // XRING) + 16)
                need(pe, S["xT_ready"], t - 1)
                for k in range(KT):
                    mm = pe.transpose(xT_ps[par][:, k * P:(k + 1) * P], x_in[u][:, k * P:(k + 1) * P], ident[:, :])
                mm.then_inc(S["xT_ps"], 1)

            def up(t, par):
                e = pe.value_load(tile_expert[0:1, bass.ds(t, 1)], min_val=0, max_val=E - 1)
                pe.wait_ge(S["xT_ready"], t + 1)
                need(pe, S["hid_a"], t - 1)
                for k in range(KT):
                    mm = pe.matmul(up_ps[par], xT[par][:, k, :],
                                   W_up[:, bass.ds(e, 1), k, :].rearrange("p a b -> p (a b)"),
                                   start=(k == 0), stop=(k == KT - 1))
                mm.then_inc(S["up_ps"], 1)

            def turn_act(t, par):
                pe.wait_ge(S["act_ready"], t + 1)
                need(pe, S["aT_ready"], t - 1)
                for k in range(KT):
                    mm = pe.transpose(aT_ps[par][:, k * P:(k + 1) * P], act_h[par][:, k * P:(k + 1) * P], ident[:, :])
                mm.then_inc(S["aT_ps"], 1)

            def down(t, par):
                e = pe.value_load(tile_expert[0:1, bass.ds(t, 1)], min_val=0, max_val=E - 1)
                pe.wait_ge(S["aT_ready"], t + 1)
                need(pe, S["y_ready2"], t - 1)
                for k in range(KT):
                    mm = pe.matmul(dn_ps[par], actT[par][:, k, :],
                                   W_dn[:, bass.ds(e, 1), k, :].rearrange("p a b -> p (a b)"),
                                   start=(k == 0), stop=(k == KT - 1))
                mm.then_inc(S["dn_ps"], 1)

            def expert(t, u):
                if not isinstance(t, int) or t + 1 < TILES:
                    turn_rows(t + 1, (u + 1) % 2, (u + 1) % XRING)
                if not isinstance(t, int) or t < TILES:
                    up(t, u % 2)
                if not isinstance(t, int) or t >= 2:
                    down(t - 2, u % 2)
                if not isinstance(t, int) or 1 <= t <= TILES:
                    turn_act(t - 1, (u + 1) % 2)

            pe.wait_ge(S["up_scaled"], KT)
            pe.wait_ge(S["expert_ready"], 1)
            turn_rows(0, 0, 0)
            sweep(pe, expert, TILES + 2, XRING, XRING + 2, XRING)

        @block.scalar
        def _(act):
            def copy(out_, in_, scale_, done, k=1):
                nc.scalar.activation(out_, in_, ACT.Copy, scale=scale_).then_inc(S[done], k)

            act.wait_ge(S["vt_ps"], 2)
            copy(VT[:, 0, :], VT_ps[:, 0:NI], 1.0, "vt_ready")
            copy(VT[:, 1, :], VT_ps[:, NI:2 * NI], 1.0, "vt_ready")
            copy(VT[:, 2, :], VT_ps[:, NI:2 * NI], -1.0, "vt_ready")

            def newton(k, c):
                act.wait_ge(S["z_ready"], k + 1)
                copy(Z[:, 2, :], Z[:, 1, :], -1.0, "zn_ready")
                act.wait_ge(S["x_ps"], k + 1)
                copy(X.rearrange("p a b -> p (a b)"), X_ps, c, "x_ready")
                act.wait_ge(S["y_ps"], k + 1)
                copy(Y[:, 0:2, :].rearrange("p a b -> p (a b)"), Y_ps, c, "y_ready")
                copy(Y[:, 2, :], Y_ps[:, NI:2 * NI], -c, "y_ready")

            with act.Fori(0, same) as k:
                newton(k, first)
            for k in range(same, len(scales)):
                newton(k, scales[k])

            act.wait_ge(S["mv_ready"], C)
            nc.scalar.activation(std[:, :], stats[:, :, 1], ACT.Sqrt, bias=eps[:, 0:1]).then_inc(S["std_ready"], 1)

            def rows_out(n, par):
                act.wait_ge(S["xt_ps"], n + 1)
                need(act, S["proj"], 4 * (n - 1))
                for t in range(KT):
                    copy(rowsT[par][:, t, :], A[:, t * L:(t + 1) * L], 1.0, "xt_ready")

            def step(n, par):
                if live(n + 1) and not (isinstance(n, int) and n + 1 >= C):
                    rows_out(n + 1, 1 - par)
                if live(n):
                    act.wait_ge(S["proj"], 4 * n + 2)
                    need(act, S["ma_ready"], n)
                    nc.scalar.activation(sq_ar, a_re, ACT.Square).then_inc(S["sqa_ready"], 1)
                    nc.scalar.activation(sq_ai, a_im, ACT.Square).then_inc(S["sqa_ready"], 1)
                    act.wait_ge(S["proj"], 4 * n + 4)
                    need(act, S["mx_ready"], n)
                    nc.scalar.activation(sq_xr, x_re, ACT.Square).then_inc(S["sqx_ready"], 1)
                    nc.scalar.activation(sq_xi, x_im, ACT.Square).then_inc(S["sqx_ready"], 1)
                    act.wait_ge(S["ma_ready"], n + 1)
                    need(act, S["srho_ready"], n)
                    need(act, S["r1_ready"], n)
                    nc.scalar.activation(rho, m_a, ACT.Sqrt, bias=tiny[:, 0:1]).then_inc(S["rho_ready"], 1)
                    need(act, S["aim_ready"], n)
                    need(act, S["prod_ready"], n)
                    nc.scalar.activation(m1, m_a, ACT.Copy, bias=1.0).then_inc(S["m1_ready"], 1)
                    act.wait_ge(S["mx_ready"], n + 1)
                    need(act, S["xc_ready"], 2 * n)
                    nc.scalar.activation(g_x, m_x, ACT.Sqrt).then_inc(S["gx_ready"], 1)
                if live(n - 1):
                    act.wait_ge(S["angle_ready"], n)
                    need(act, S["back_ready"], 4 * (n - 2))
                    nc.scalar.activation(mag, angle, ACT.Abs, scale=2.0).then_inc(S["mag_ready"], 1)
                    nc.scalar.activation(sinE[1 - par], angle, ACT.Sin, scale=2.0).then_inc(S["sin_ready"], 1)
                    act.wait_ge(S["mag_ready"], n)
                    nc.scalar.activation(cosE[1 - par], mag, ACT.Sin, scale=-1.0,
                                         bias=half_pi[:, 0:1]).then_inc(S["cos_ready"], 1)
                if live(n):
                    act.wait_ge(S["tan_ready"], n + 1)
                    need(act, S["phi_ready"], n)
                    nc.scalar.activation(half, tan_h, ACT.Arctan).then_inc(S["atan_ready"], 1)

            rows_out(0, 0)
            sweep(act, step, C + 2, 4, 4)

            act.wait_ge(S["mv2_ready"], C)
            nc.scalar.activation(std2[:, 0, :], stats2[:, :, 1], ACT.Sqrt, bias=eps[:, 0:1]).then_inc(S["r_std"], 1)
            act.wait_ge(S["r_c"], 1)
            nc.scalar.activation(std2[:, 1, :], rstd2[:, 2, :], ACT.Sqrt, bias=eps[:, 0:1]).then_inc(S["r_d"], 1)
            act.wait_ge(S["gate_in"], 64)

            def routing(c, par):
                if not isinstance(c, int) or c > 0:
                    act.wait_ge(S["rT_ps"], c)
                    need(act, S["bd_ps"], c - 1)
                    copy(routeT[:, :], rT_ps, 1.0, "rT_ready")
                if not isinstance(c, int) or c < C:
                    act.wait_ge(S["tT_ps"], c + 1)
                    need(act, S["gate_ps"], c - 1)
                    for t in range(KT):
                        nc.scalar.activation(tT[par][:, t, :], A[:, t * L:(t + 1) * L], ACT.Copy,
                                             scale=scale_col[:, t:t + 1]).then_inc(S["tT_ready"], 1)
                    act.wait_ge(S["diff_ready"], c + 1)
                    need(act, S["expm_ready"], c)
                    nc.scalar.activation(expd[:, :, :], expd[:, :, :], ACT.Exp).then_inc(S["exp_ready"], 1)

            sweep(act, routing, C + 1, 2, 1)

            def expert(t, u):
                if not isinstance(t, int) or t + 1 < TILES:
                    act.wait_ge(S["xT_ps"], t + 2)
                    need(act, S["up_ps"], t)
                    copy(xT[(u + 1) % 2].rearrange("p a b -> p (a b)"), xT_ps[(u + 1) % 2], 1.0, "xT_ready")
                if not isinstance(t, int) or t < TILES:
                    act.wait_ge(S["hid_ready"], t + 1)
                    need(act, S["aT_ps"], t - 1)
                    nc.scalar.activation(act_h[u % 2], hid[u % 2], ACT.Gelu_apprx_sigmoid)\
                        .then_inc(S["act_ready"], 1)
                if not isinstance(t, int) or 1 <= t <= TILES:
                    act.wait_ge(S["aT_ps"], t)
                    need(act, S["dn_ps"], t - 2)
                    copy(actT[(u + 1) % 2].rearrange("p a b -> p (a b)"), aT_ps[(u + 1) % 2], 1.0, "aT_ready")

            act.wait_ge(S["xT_ps"], 1)
            copy(xT[0].rearrange("p a b -> p (a b)"), xT_ps[0], 1.0, "xT_ready")
            sweep(act, expert, TILES + 1, XRING, XRING + 1, XRING)

        @block.vector
        def _(dve):
            steps = [0]

            def link(ins):
                steps[0] += 1
                ins.then_inc(S["dve_step"], 1)
                dve.wait_ge(S["dve_step"], steps[0])

            dve.wait_ge(S["v_in"], 32)
            link(dve.tensor_tensor_reduce(sq_junk, v_nat[:, 0, :], v_nat[:, 0, :], 1.0, 0.0, ALU.mult, ALU.add,
                                     frob[:, 0:1]))
            link(dve.tensor_tensor_reduce(sq_junk, v_nat[:, 1, :], v_nat[:, 1, :], 1.0, 0.0, ALU.mult, ALU.add,
                                     frob[:, 1:2]))
            dve.tensor_tensor(frob[:, 2:3], frob[:, 0:1], frob[:, 1:2], ALU.add).then_inc(S["frob_sum"], 1)
            dve.wait_ge(S["frob_ps"], 1)
            link(dve.reciprocal(frob[:, 3:4], N_ps[:, 0:1]))
            dve.tensor_scalar(Y[:, 0, :], v_nat[:, 0, :], frob[:, 3:4], None, ALU.mult).then_inc(S["y0_ready"], 1)
            dve.tensor_scalar(Y[:, 1, :], v_nat[:, 1, :], frob[:, 3:4], -1.0, ALU.mult, ALU.mult)\
                .then_inc(S["y0_ready"], 1)
            dve.tensor_scalar(Y[:, 2, :], v_nat[:, 1, :], frob[:, 3:4], None, ALU.mult).then_inc(S["y0_ready"], 1)
            dve.wait_ge(S["vt_ready"], 3)
            dve.tensor_scalar(X[:, 0, :], VT[:, 0, :], frob[:, 3:4], None, ALU.mult).then_inc(S["x0_ready"], 1)
            dve.tensor_scalar(X[:, 1, :], VT[:, 2, :], frob[:, 3:4], None, ALU.mult).then_inc(S["x0_ready"], 1)

            def newton(k, c):
                dve.wait_ge(S["t_ps"], k + 1)
                dve.scalar_tensor_tensor(Z[:, 0:2, :].rearrange("p a b -> p (a b)"), T_ps, -c,
                                         two_i.rearrange("p a b -> p (a b)"), ALU.mult, ALU.add)\
                    .then_inc(S["z_ready"], 1)

            def embed(c, par):
                dve.wait_ge(gathered[par], ((c - par) // 2 + 1) * 16 * TPC if isinstance(c, int)
                            else (c - par + 2) * 8 * TPC)
                dve.tensor_tensor(H[:, bass.ds(c * TPC, TPC), :], rows[par], bias_rows, ALU.add)\
                    .then_inc(S["h_ready"], 1)
                dve.wait_ge(S["h_ready"], c + 1)
                apart(dve)
                for i in range(TPC):
                    dve.bn_stats(st6[:, i, :], H[:, bass.ds(c * TPC + i, 1), :].rearrange("p a b -> p (a b)"))\
                        .then_inc(S["st_ready"], 1)
                for i in range(TPC):
                    dve.wait_ge(S["st_ready"], c * TPC + i + 1)
                    if i == 0:
                        need(dve, S["mv_ready"], c)
                    apart(dve)
                    dve.bn_aggr(mv[:, i, :], st6[:, i, :]).then_inc(S["ag_ready"], 1)
                dve.wait_ge(S["ag_ready"], TPC * (c + 1))
                dve.tensor_copy(stats[:, bass.ds(c * TPC, TPC), :], mv[:, :, :]).then_inc(S["mv_ready"], 1)

            def early(k, par):
                if isinstance(k, int) and k == 0:
                    dve.wait_ge(S["bias_in"], 16 * TPC)
                newton(k, first)
                embed(k, par)

            sweep(dve, early, C, 2, 0)
            with dve.Fori(C, same) as k:
                newton(k, first)
            for k in range(same, len(scales)):
                newton(k, scales[k])

            dve.wait_ge(S["std_ready"], 1)
            dve.reciprocal(rstd[:, :], std[:, :]).then_inc(S["rstd_ready"], 1)
            dve.wait_ge(S["rstd_ready"], 1)

            def normed(n, par):
                need(dve, S["xt_ps"], n - 1)
                for i in range(TPC):
                    j = n * TPC + i
                    dve.tensor_scalar(rows[par][:, i, :], H[:, bass.ds(j, 1), :].rearrange("p a b -> p (a b)"),
                                      stats[:, bass.ds(j, 1), 0], rstd[:, bass.ds(j, 1)],
                                      ALU.subtract, ALU.mult).then_inc(S["xn_ready"], 1)

            normed(0, 0)
            normed(1, 1)
            dve.wait_ge(S["y_ready"], 2 * len(scales))
            dve.wait_ge(S["const_set"], 10)
            dve.wait_ge(S["h0_in"], 64)

            def phase(n):
                dve.wait_ge(S["atan_ready"], n + 1)
                dve.tensor_tensor_scan(phi[:, 1:L + 1], half, zeros, 0.0, ALU.add, ALU.add)\
                    .then_inc(S["phi_ready"], 1)
                dve.wait_ge(S["phi_ready"], n + 1)
                dve.tensor_scalar(turns, phi[:, 1:L + 1], 1 / PI, MAGIC, ALU.mult, ALU.add)\
                    .then_inc(S["turns_ready"], 1)
                dve.wait_ge(S["turns_ready"], n + 1)
                need(dve, S["sum_ready"], n)
                dve.tensor_scalar(turns, turns, MAGIC, -PI, ALU.subtract, ALU.mult).then_inc(S["npi_ready"], 1)
                dve.wait_ge(S["npi_ready"], n + 1)
                need(dve, S["mag_ready"], n)
                need(dve, S["sin_ready"], n)
                dve.tensor_tensor(angle[:, 1:L + 1], phi[:, 1:L + 1], turns, ALU.add).then_inc(S["sum_ready"], 1)
                dve.wait_ge(S["sum_ready"], n + 1)
                if isinstance(n, int) and n == 0:
                    dve.tensor_copy(angle[:, 0:1], phi[:, 0:1])
                dve.tensor_scalar(angle[:, 1:L + 1], angle[:, 1:L + 1], PI / 2, -PI / 2, ALU.min, ALU.max)\
                    .then_inc(S["angle_ready"], 1)

            def scans(n, par):
                dve.wait_ge(S["w_ready"], 2 * n + 2)
                dve.wait_ge(S["decay_ready"], n + 1)
                dve.tensor_tensor_scan(z_re, w_re, decay[par], 0.0, ALU.add, ALU.mult).then_inc(S["z_ready2"], 1)
                dve.tensor_tensor_scan(z_im, w_im, decay[par], 0.0, ALU.add, ALU.mult).then_inc(S["z_ready2"], 1)
                cs, sn = cosE[par][:, 1:L + 1], sinE[par][:, 1:L + 1]
                for out_, a, b, k in ((c_zr, cs, z_re, 1), (s_zi, sn, z_im, 2), (s_zr, sn, z_re, 2),
                                      (c_zi, cs, z_im, 2)):
                    dve.wait_ge(S["z_ready2"], 2 * n + k)
                    dve.tensor_tensor(out_, a, b, ALU.mult).then_inc(S["back_ready"], 1)

            def polar(n):
                dve.wait_ge(S["proj"], 4 * n + 2)
                dve.wait_ge(S["rho_ready"], n + 1)
                need(dve, S["r1_ready"], n)
                dve.scalar_tensor_tensor(srho.bitcast(U32), a_re.bitcast(U32), 0x80000000, rho.bitcast(U32),
                                         ALU.bitwise_and, ALU.bitwise_or).then_inc(S["srho_ready"], 1)
                dve.wait_ge(S["m1_ready"], n + 1)
                dve.tensor_tensor(aim, a_im, m1, ALU.mult).then_inc(S["aim_ready"], 1)
                dve.wait_ge(S["srho_ready"], n + 1)
                need(dve, S["r2_ready"], n)
                dve.tensor_tensor(den, a_re, srho, ALU.add).then_inc(S["den_ready"], 1)
                dve.wait_ge(S["den_ready"], n + 1)
                dve.tensor_tensor(prod, den, m1, ALU.mult).then_inc(S["prod_ready"], 1)
                dve.wait_ge(S["prod_ready"], n + 1)
                need(dve, S["decay_ready"], n)
                dve.reciprocal(rec, prod).then_inc(S["rec_ready"], 1)
                dve.wait_ge(S["rec_ready"], n + 1)
                dve.wait_ge(S["aim_ready"], n + 1)
                dve.tensor_tensor(tan_h, aim, rec, ALU.mult).then_inc(S["tan_ready"], 1)

            def add_x(n, par):
                dve.wait_ge(S["hr_ps"], n + 1)
                need(dve, S["o_ps"], n)
                dve.tensor_tensor(h_re, A[:, 0:L], xc_re[par][:, 1:L + 1], ALU.add).then_inc(S["h_re_ready"], 1)

            def inputs(n, par):
                dve.wait_ge(S["proj"], 4 * n + 4)
                dve.wait_ge(S["gx_ready"], n + 1)
                need(dve, S["u_ps"], n - 1)
                need(dve, S["h_re_ready"], n - 1)
                dve.tensor_tensor(xc_re[par][:, 1:L + 1], x_re, g_x, ALU.mult).then_inc(S["xc_ready"], 1)
                dve.tensor_tensor(xc_im[par][:, 1:L + 1], x_im, g_x, ALU.mult).then_inc(S["xc_ready"], 1)

            def turn(n, par):
                dve.wait_ge(S["u_ps"], n + 1)
                dve.wait_ge(S["cos_ready"], n + 1)
                dve.wait_ge(S["sin_ready"], n + 1)
                need(dve, S["s_ready"], 2 * n)
                cs, sn = cosE[par][:, 0:L], sinE[par][:, 0:L]
                for out_, a, b in ((c_ur, cs, u_re), (s_ui, sn, u_im), (c_ui, cs, u_im), (s_ur, sn, u_re)):
                    dve.tensor_tensor(out_, a, b, ALU.mult).then_inc(S["rot_ready"], 1)

            def residual(n):
                dve.wait_ge(S["o_ps"], n + 1)
                hs = H[:, bass.ds(n * TPC, TPC), :]
                dve.tensor_tensor(hs, A[:, :].rearrange("p (a b) -> p a b", a=TPC), hs, ALU.add)\
                    .then_inc(S["h2_ready"], 1)

            def spread(n):
                dve.wait_ge(S["h2_ready"], n + 1)
                apart(dve)
                for i in range(TPC):
                    dve.bn_stats(st6[:, i, :], H[:, bass.ds(n * TPC + i, 1), :].rearrange("p a b -> p (a b)"))\
                        .then_inc(S["stat2_ready"], 1)
                for i in range(TPC):
                    dve.wait_ge(S["stat2_ready"], n * TPC + i + 1)
                    if i == 0:
                        need(dve, S["mv2_ready"], n)
                    apart(dve)
                    dve.bn_aggr(mv[:, i, :], st6[:, i, :]).then_inc(S["ag2_ready"], 1)
                dve.wait_ge(S["ag2_ready"], TPC * (n + 1))
                dve.tensor_copy(stats2[:, bass.ds(n * TPC, TPC), :], mv[:, :, :]).then_inc(S["mv2_ready"], 1)

            def step(n, par):
                if live(n - 1):
                    phase(n - 1)
                if live(n - 2):
                    scans(n - 2, par)
                if live(n):
                    polar(n)
                if live(n - 2):
                    add_x(n - 2, par)
                if live(n):
                    inputs(n, par)
                if live(n - 1):
                    turn(n - 1, 1 - par)
                if live(n - 2):
                    residual(n - 2)
                    spread(n - 2)
                if live(n + 2) and not (isinstance(n, int) and n + 2 >= C):
                    normed(n + 2, par)

            sweep(dve, step, C + 2, 4, 4)

            dve.wait_ge(S["r_std"], 1)
            link(dve.reciprocal(rstd2[:, 0, :], std2[:, 0, :]))
            link(dve.tensor_tensor(rstd2[:, 1, :], rstd2[:, 0, :], rstd2[:, 0, :], ALU.mult))
            dve.tensor_tensor(rstd2[:, 2, :], rstd2[:, 1, :], stats2[:, :, 1], ALU.mult).then_inc(S["r_c"], 1)
            dve.wait_ge(S["r_d"], 1)
            link(dve.reciprocal(rstd2[:, 1, :], std2[:, 1, :]))
            link(dve.tensor_tensor(rstd2[:, 3, :], rstd2[:, 0, :], rstd2[:, 1, :], ALU.mult))
            dve.wait_ge(S["gate_in"], 64)
            dve.wait_ge(S["iota_ready"], 14)

            def normed2(c, par):
                need(dve, S["rT_ps"], c - 1)
                need(dve, table_in[par], (c - par) * 8)
                need(dve, S["part_ready"], TPC * (c - 1))
                for i in range(TPC):
                    j = c * TPC + i
                    dve.tensor_scalar(entry[par][:, i, 0:D], H[:, bass.ds(j, 1), :].rearrange("p a b -> p (a b)"),
                                      stats2[:, bass.ds(j, 1), 0], rstd2[:, 3, bass.ds(j, 1)],
                                      ALU.subtract, ALU.mult).then_inc(S["entry_ready"], 1)

            def choose(c, par):
                dve.wait_ge(S["gate_ps"], c + 1)
                need(dve, S["diff_ready"], c)
                dve.tensor_tensor(logit[:, :, 0:E], logit_ps.rearrange("p (a b) -> p a b", a=TPC),
                                  gate_bias[:, :].unsqueeze(1).to_broadcast([P, TPC, E]), ALU.add)\
                    .then_inc(S["logit_ready"], 1)
                dve.wait_ge(S["logit_ready"], c + 1)
                apart(dve)
                for i in range(TPC):
                    dve.max(top8[:, i, :], logit[:, i, 0:E]).then_inc(S["top8_ready"], 1)
                dve.wait_ge(S["top8_ready"], TPC * (c + 1))
                dve.tensor_copy(top4[:, :, 0:K], top8[:, :, 0:K]).then_inc(S["top4_ready"], 1)
                need(dve, S["exp_ready"], c)
                need(dve, S["expm_ready"], c)
                dve.tensor_tensor(expd[:, :, :], logit[:, :, 0:E], top8[:, :, 0:1].to_broadcast([P, TPC, E]),
                                  ALU.subtract).then_inc(S["diff_ready"], 1)
                dve.wait_ge(S["top4_ready"], c + 1)
                apart(dve)
                for i in range(TPC):
                    dve.match_replace(left[:, i, :], top4[:, i, :], logit[:, i, :], -BIG)\
                        .then_inc(S["left_ready"], 1)
                dve.wait_ge(S["left_ready"], TPC * (c + 1))
                m = mask[:, bass.ds(c * TPC * E, TPC * E)].rearrange("p (a b) -> p a b", a=TPC)
                dve.tensor_tensor(m, left[:, :, 0:E], logit[:, :, 0:E], ALU.not_equal).then_inc(S["mask_ready"], 1)
                dve.wait_ge(S["mask_ready"], c + 1)
                dve.wait_ge(S["exp_ready"], c + 1)
                dve.tensor_tensor(expm[:, :, :], expd[:, :, :], m, ALU.mult).then_inc(S["expm_ready"], 1)
                dve.wait_ge(S["expm_ready"], c + 1)
                dve.tensor_reduce(sums[:, 0, :], expm[:, :, :], AXX, ALU.add).then_inc(S["esum_ready"], 1)
                dve.wait_ge(S["esum_ready"], c + 1)
                dve.reciprocal(sums[:, 1, :], sums[:, 0, :]).then_inc(S["erec_ready"], 1)
                dve.wait_ge(S["erec_ready"], c + 1)
                dve.tensor_tensor(entry[par][:, :, D:D + E], expm[:, :, :],
                                  sums[:, 1, :].unsqueeze(2).to_broadcast([P, TPC, E]), ALU.mult)\
                    .then_inc(S["route_ready"], 1)

            def start_sum(c, par):
                dve.wait_ge(S["bd_ps"], c + 1)
                need(dve, acc_in[par], (c - par) * 8)
                for i in range(TPC):
                    dve.scalar_tensor_tensor(acc_row[par][:, i, :], entry[par][:, i, 0:D],
                                             std2[:, 1, bass.ds(c * TPC + i, 1)], Cb[:, i * D:(i + 1) * D],
                                             ALU.mult, ALU.add).then_inc(S["part_ready"], 1)

            def routing(c, par):
                if not isinstance(c, int) or c > 0:
                    start_sum(c - 1, 1 - par)
                if not isinstance(c, int) or c + 1 < C:
                    normed2(c + 1, 1 - par)
                if not isinstance(c, int) or c < C:
                    choose(c, par)

            normed2(0, 0)
            sweep(dve, routing, C + 1, 4, 3)

            ej = "p (e j) -> p e j"
            je = "p (j e) -> p e j"
            for i in range(2):
                dve.wait_ge(table_in[i], 8 * C)
                dve.wait_ge(acc_in[i], 8 * C)
            dve.wait_ge(S["totps"], 2)
            link(dve.tensor_copy(total.rearrange(ej, e=E), Cb[:, :].rearrange(je, e=E)))
            link(dve.tensor_tensor_scan(upto, keep[:, 0, :], total, 0.0, ALU.mult, ALU.add))
            link(dve.tensor_tensor(total, upto, total, ALU.subtract))
            counts = upto.rearrange(ej, e=E)[:, :, NT - 1]
            link(dve.tensor_scalar(tiles_e[:, 0, :], counts, 1.0 / P, (P - 1) / (2.0 * P), ALU.mult, ALU.add))
            link(dve.tensor_scalar(tiles_e[:, 1, :], tiles_e[:, 0, :], MAGIC, -MAGIC, ALU.add, ALU.add))
            link(dve.tensor_tensor_scan(tiles_e[:, 2, :], tiles_e[:, 1, :], found[:, 0, 0:E], 0.0, ALU.add, ALU.add))
            link(dve.tensor_tensor(tiles_e[:, 3, :], tiles_e[:, 2, :], tiles_e[:, 1, :], ALU.subtract))
            dve.wait_ge(S["lowps"], 2)
            sj = slot.rearrange("p (j e) -> p j e", e=E)
            link(dve.tensor_tensor(sj, A[:, :].rearrange("p (j e) -> p j e", e=E),
                              total.rearrange("p (e j) -> p j e", e=E), ALU.add))
            link(dve.scalar_tensor_tensor(sj, tiles_e[:, 3, :].unsqueeze(1).to_broadcast([P, NT, E]), float(P), sj,
                                     ALU.mult, ALU.add))
            link(dve.tensor_tensor_scan(order, keep[:, 1, :], mask[:, :], 0.0, ALU.mult, ALU.add))
            link(dve.tensor_tensor(order, order, mask[:, :], ALU.mult))
            for k in range(K):
                link(dve.scalar_tensor_tensor(picked, order, float(k + 1), slot, ALU.is_equal, ALU.mult))
                link(dve.tensor_reduce(slots[:, :].rearrange("p (j k) -> p j k", k=K)[:, :, k],
                                  picked.rearrange("p (j e) -> p j e", e=E), AXX, ALU.add))
            link(dve.tensor_copy(slots_i[:, 0, :], slots[:, :]))
            link(dve.tensor_scalar(slots_i[:, 1, :], slots_i[:, 0, :], P - 1, None, ALU.bitwise_and))
            link(dve.tensor_scalar(slots_i[:, 2, :], slots_i[:, 0, :], 7, None, ALU.arith_shift_right))
            dve.tensor_copy(slot_lo[:, :], slots_i[:, 1, :]).then_inc(S["slot_ready"], 1)
            dve.tensor_copy(slot_hi[:, :], slots_i[:, 2, :]).then_inc(S["slot_ready"], 1)
            dve.wait_ge(S["slot_ready"], 2)

            def put(q, j, par):
                need(dve, S["hot_used"], q - HOTS + 1)
                dve.tensor_scalar(hot_lo[par][:, :], iota_lo[:, :], slot_lo[:, bass.ds(q, 1)], None,
                                  ALU.is_equal).then_inc(S["hotlo_ready"], 1)
                dve.tensor_scalar(hot_hi[par][:, :], iota_hi[:, :], slot_hi[:, bass.ds(q, 1)],
                                  value[:, bass.ds(j, 1)], ALU.is_equal, ALU.mult).then_inc(S["hothi_ready"], 1)

            per = NT // QUARTERS
            for f in range(QUARTERS):
                if f == 0:
                    for k in range(K):
                        put(k, 0, k)
                with dve.Fori(1 if f == 0 else 0, per) as j:
                    for k in range(K):
                        put((f * per + j) * K + k, j, k)

            dve.wait_ge(S["hothi_ready"], NT * K)
            link(dve.tensor_scalar(expert_f[:, 0, :], iota_tf[:, :], tiles_e[:, 2, 0:1], None, ALU.is_ge))
            for e in range(1, E):
                link(dve.scalar_tensor_tensor(expert_f[:, e % 2, :], iota_tf[:, :], tiles_e[:, 2, e:e + 1],
                                         expert_f[:, (e - 1) % 2, :], ALU.is_ge, ALU.add))
            last = (E - 1) % 2
            dve.tensor_scalar(tile_expert[:, :], expert_f[:, last, :], float(E - 1), None, ALU.min)\
                .then_inc(S["expert_ready"], 1)
            link(dve.tensor_tensor(expert_f[:, 1 - last, 1:TILES], expert_f[:, last, 1:TILES],
                              expert_f[:, last, 0:TILES - 1], ALU.not_equal))
            link(dve.tensor_copy(expert_f[:, 1 - last, 0:1], expert_f[:, last, 0:1]))
            link(dve.tensor_scalar(expert_f[:, 2, :], expert_f[:, last, :], float(E), None, ALU.is_ge))
            dve.tensor_tensor(tile_starts[:, :], expert_f[:, 1 - last, :], expert_f[:, 2, :], ALU.max)\
                .then_inc(S["expert_ready"], 1)

            dve.wait_ge(S["hot_used"], NT * K)
            link(dve.tensor_copy(found[:, 1, :], B[:, 0:TILES]))
            for f in range(1, QUARTERS):
                bank = B[:, f * L:f * L + TILES]
                link(dve.tensor_scalar(found[:, 2, :], bank, 0.0, float(f * per * P), ALU.is_gt, ALU.mult))
                link(dve.tensor_tensor(found[:, 1, :], found[:, 1, :], found[:, 2, :], ALU.add))
                link(dve.tensor_tensor(found[:, 1, :], found[:, 1, :], bank, ALU.add))
            link(dve.tensor_scalar(sums[:, 0, 0:1], value[:, 0:1], float(NT * P), None, ALU.add))
            link(dve.tensor_scalar(found[:, 2, :], found[:, 1, :], 0.0, sums[:, 0, 0:1], ALU.is_equal, ALU.mult))
            dve.scalar_tensor_tensor(slot_token[:, :], found[:, 1, :], -1.0, found[:, 2, :], ALU.add, ALU.add)\
                .then_inc(S["tok_ready"], 1)

            def hidden(t, par):
                e = dve.value_load(tile_expert[0:1, bass.ds(t, 1)], min_val=0, max_val=E - 1)
                dve.wait_ge(S["up_ps"], t + 1)
                need(dve, S["act_ready"], t - 1)
                dve.tensor_tensor(hid[par], up_ps[par], b_up[:, bass.ds(e, 1), :].rearrange("p a b -> p (a b)"),
                                  ALU.add).then_inc(S["hid_a"], 1)
                dve.wait_ge(S["hid_a"], t + 1)
                dve.tensor_scalar(hid[par], hid[par], LIMIT, None, ALU.min).then_inc(S["hid_ready"], 1)

            def weigh(t, u):
                e = dve.value_load(tile_expert[0:1, bass.ds(t, 1)], min_val=0, max_val=E - 1)
                dve.wait_ge(S["dn_ps"], t + 1)
                need(dve, scattered[u % RING], bound(t, u % RING))
                dve.tensor_scalar(y_out[u % RING], dn_ps[u % 2], x_in[u][:, bass.ds(e + D, 1)], LIMIT + 1.0,
                                  ALU.mult, ALU.mult).then_inc(S["y_ready2"], 1)

            def expert(t, u):
                if not isinstance(t, int) or t < TILES:
                    hidden(t, u % 2)
                if not isinstance(t, int) or t >= 2:
                    weigh(t - 2, (u - 2) % XRING)

            dve.wait_ge(S["weights_in"], 16 * (2 * KT + 1))
            sweep(dve, expert, TILES + 2, XRING, 2, XRING)


def layout(i):
    import numpy as np

    c = np.ascontiguousarray
    g = lambda n: np.asarray(i[n])
    inner, width = g("L0_attn_mat_v_real").shape[0], g("L0_tok_W").shape[0]
    E = g("L0_ffn_gate_b").shape[0]
    m1 = g("L0_ffn_mlp1_w")
    return {
        "x": c(g("x").reshape(-1, 128).T),
        "tok_W": c(g("L0_tok_W").T),
        "tok_b": c(g("L0_tok_b")),
        "w_a": c(g("L0_attn_w_a").reshape(inner, 2, width).transpose(2, 1, 0)),
        "w_x": c(g("L0_attn_w_x").reshape(inner, 2, width).transpose(2, 1, 0)),
        "w_out": c(g("L0_attn_w_out").T),
        "v_re": c(g("L0_attn_mat_v_real")),
        "v_im": c(g("L0_attn_mat_v_imag")),
        "h0_re": c(g("L0_attn_last_hidden_real").reshape(-1, 1)),
        "h0_im": c(g("L0_attn_last_hidden_imag").reshape(-1, 1)),
        "scale": c(g("L0_ffn_scale").reshape(-1, 128).T),
        "gate_w": c(g("L0_ffn_gate_w").T),
        "gate_b": c(g("L0_ffn_gate_b")),
        "mlp1_w": c(m1.reshape(E, -1, 2, width).transpose(0, 3, 2, 1)),
        "mlp1_b": c(g("L0_ffn_mlp1_b").reshape(E, -1, 2).transpose(0, 2, 1)),
        "mlp2_w": c(g("L0_ffn_mlp2_w").transpose(0, 2, 1)),
        "mlp2_b": c(g("L0_ffn_mlp2_b")),
    }


def kernel(**inputs):
    import concourse.bacc as bacc
    from concourse.bass_utils import run_bass_kernel_spmd

    arrays = layout(inputs)
    batch, seq = inputs["x"].shape
    width = inputs["L0_tok_W"].shape[0]
    nc = bacc.Bacc("TRN2", target_bir_lowering=False, num_devices=1)
    args = [nc.dram_tensor(n, a.shape, mybir.dt.from_np(a.dtype), kind="ExternalInput").ap()
            for n, a in arrays.items()]
    out = nc.dram_tensor("out", (batch * seq + 128, width), F32, kind="ExternalOutput").ap()
    layer_kernel(nc, *args, out)
    r = run_bass_kernel_spmd(nc, [arrays], core_ids=[0])
    return r.results[0]["out"][:batch * seq].reshape(batch, seq, width)
```
